# Optimizing a Trainium2 kernel written in Bass

```python
import numpy as np
import jax
import jax.numpy as jnp

def _softmax(x, axis=-1):
    return jax.nn.softmax(x, axis=axis)

def _gelu(x):
    return jax.nn.gelu(x, approximate=True)

def _silu(x):
    return jax.nn.silu(x)

def _sigmoid(x):
    return jax.nn.sigmoid(x)

def _layernorm(x, axis=-1, eps=1e-05):
    m = jnp.mean(x, axis=axis, keepdims=True)
    v = jnp.var(x, axis=axis, keepdims=True)
    return (x - m) / jnp.sqrt(v + eps)

def _scatter_add(tgt, idx, src, axis=0):
    return tgt.at[idx].add(src)

def _segment_sum(src, seg, n):
    return jax.ops.segment_sum(src, seg, n)
kernel_name = 'mk_adj_resnorm_d1_adj_r2_240e25'

def setup_inputs(seed: int=0):
    np.random.seed(seed)
    _w = jnp.asarray

    def _rec_inputs():
        import jax
        import jax.numpy as jnp
        _gk = jax.random.key(seed)
        x = -0.0002928 + 1 * jax.random.normal(jax.random.fold_in(_gk, 1), (3327, 512), jnp.float32)
        _w = (1.0 + jnp.arange(3327, dtype=jnp.float32)) ** (-0.5)
        _w = _w / _w.mean()
        _pij = jnp.clip(0.00120228 * _w[:, None] * _w[None, :], 0.0, 1.0)
        _a = jax.random.uniform(jax.random.fold_in(_gk, 2), (3327, 3327)) < _pij
        _af = _a.astype(jnp.float32)
        adj = _af
        return (x, adj)
    x, adj = _rec_inputs()

    def _L0_gnn_setup():
        import jax, jax.numpy as jnp
        import numpy as np
        import math
        SENT_DIM = 512
        N_SENT = 2048
        key = jax.random.key(seed)
        ks = jax.random.split(key, 8)
        D = SENT_DIM
        s = 1.0 / math.sqrt(D)
        return {'sent_embed': jax.random.normal(ks[0], (N_SENT, D), dtype=jnp.float32), 'adj_tensor': jax.random.randint(ks[1], (N_SENT, N_SENT), 0, 2).astype(jnp.float32), 'W_q': jax.random.uniform(ks[2], (D, D), jnp.float32, -s, s), 'b_q': jax.random.uniform(ks[3], (D,), jnp.float32, -s, s), 'W_k': jax.random.uniform(ks[4], (D, D), jnp.float32, -s, s), 'b_k': jax.random.uniform(ks[5], (D,), jnp.float32, -s, s), 'W_v': jax.random.uniform(ks[6], (D, D), jnp.float32, -s, s), 'b_v': jax.random.uniform(ks[7], (D,), jnp.float32, -s, s)}
    _L0_gnn_all = _L0_gnn_setup()
    _L0_gnn_in = {k: v for k, v in _L0_gnn_all.items() if k in ('W_q', 'b_q', 'W_k', 'b_k', 'W_v', 'b_v')}
    del _L0_gnn_all
    return {'x': x, 'adj': adj, 'L0_gnn_W_q': _L0_gnn_in['W_q'], 'L0_gnn_b_q': _L0_gnn_in['b_q'], 'L0_gnn_W_k': _L0_gnn_in['W_k'], 'L0_gnn_b_k': _L0_gnn_in['b_k'], 'L0_gnn_W_v': _L0_gnn_in['W_v'], 'L0_gnn_b_v': _L0_gnn_in['b_v']}

def reference(x, adj, L0_gnn_W_q, L0_gnn_b_q, L0_gnn_W_k, L0_gnn_b_k, L0_gnn_W_v, L0_gnn_b_v):
    import jax
    import jax.numpy as jnp

    def _L0_gnn_ref(sent_embed, adj_tensor, W_q, b_q, W_k, b_k, W_v, b_v):
        import jax, jax.numpy as jnp
        import numpy as np
        import math
        SENT_DIM = 512
        N_SENT = 2048
        q = sent_embed @ W_q.T + b_q
        k = sent_embed @ W_k.T + b_k
        v = sent_embed @ W_v.T + b_v
        scale = 1.0 / math.sqrt(sent_embed.shape[-1])
        z = scale * (q @ k.T)
        spare_z = z * adj_tensor
        spare_z = jnp.where(spare_z == 0.0, jnp.asarray(-10000.0, spare_z.dtype), spare_z)
        attn = jax.nn.softmax(spare_z, axis=1)
        out = attn @ v
        return jax.nn.relu(out)
    x = _layernorm(x + _L0_gnn_ref(x, adj, L0_gnn_W_q, L0_gnn_b_q, L0_gnn_W_k, L0_gnn_b_k, L0_gnn_W_v, L0_gnn_b_v), axis=-1)
    return x

_drawn_inputs = setup_inputs


def setup_inputs(seed=0):
    import zlib

    import numpy as np

    out = dict(_drawn_inputs(seed))
    spreads = {}
    factors = {'L0_gnn_b_q': 28.826, 'L0_gnn_b_k': 64.0, 'L0_gnn_b_v': 3.276}
    for name, (base, spread) in spreads.items():
        noise = np.random.default_rng([zlib.crc32(name.encode()), seed]).standard_normal(out[name].shape)
        drawn = base * np.exp(spread * noise) if base else spread * noise
        out[name] = jnp.asarray(drawn.astype(out[name].dtype))
    for name, factor in factors.items():
        out[name] = (out[name] * factor).astype(out[name].dtype)
    return out
```

```python
import math

import concourse.bass as bass
from concourse import mybir
from contextlib import ExitStack

P = 128


def graph_attention_kernel(nc, x, adj, w_q, b_q, w_k, b_k, w_v, b_v, out):
    f32, f16 = mybir.dt.float32, mybir.dt.float16
    ALU, ACT, AX = mybir.AluOpType, mybir.ActivationFunctionType, mybir.AxisListType

    N, D = x.shape
    KD = D // P
    TILES = -(-N // P)
    LAST_ROWS = N - (TILES - 1) * P
    PAIRS = TILES // 2
    NP = TILES * P
    BLK = 512
    BLOCKS = -(-N // BLK)
    width = [min(BLK, N - b * BLK) for b in range(BLOCKS)]
    chunks = [-(-w // P) for w in width]
    STEPS = 2 * BLOCKS
    LAG_E, LAG_T, LAG_V = BLOCKS, BLOCKS + 1, BLOCKS + 2
    LAG_N = LAG_V + BLOCKS
    G_STEP = BLOCKS + 1
    assert TILES % 2 == 0 and BLOCKS % 2 == 1 and D == BLK

    WV_SCALE, V_SCALE, A_SCALE, G_SCALE = 2.0 ** 8, 2.0 ** 4, 2.0 ** 10, 2.0 ** 4
    FILL = 10000.0
    KAPPA = 1.0 / (math.sqrt(D) * FILL * G_SCALE)
    P_SHIFT = 13 * math.log(2.0)
    EPS = 1e-5

    ctx = ExitStack()
    with ctx:
        def sbuf(name, shape, dt):
            return ctx.enter_context(nc.sbuf_tensor(name, shape, dt))

        def sem(name):
            return ctx.enter_context(nc.semaphore(name))

        xT = sbuf("xT", [P, KD, 2, NP], f16)
        V = sbuf("V", [P, TILES, 2, D], f16)
        A = sbuf("A", [P, KD, 2, D], f16)
        r_all = sbuf("r_all", [P, TILES], f32)
        bv_rows = sbuf("bv_rows", [P, D], f32)
        identity = sbuf("identity", [P, P], f32)
        g_bias = sbuf("g_bias", [P, KD], f32)
        minus_half = sbuf("minus_half", [P, 1], f32)
        adj_t = [sbuf(f"adj_t{i}", [P, NP], f32) for i in range(2)]
        probs = [sbuf(f"probs{i}", [P, NP], f32) for i in range(2)]
        x_in = [sbuf(f"x_in{i}", [P, D], f32) for i in range(2)]
        y = [sbuf(f"y{i}", [P, D], f32) for i in range(2)]
        G = [sbuf(f"G{i}", [P, KD, 2, P], f16) for i in range(2)]
        exp_bias = [sbuf(f"exp_bias{i}", [P, 1], f32) for i in range(2)]
        sums = [sbuf(f"sums{i}", [P, BLOCKS], f32) for i in range(2)]
        pT = [sbuf(f"pT{i}", [P, 2, BLK], f16) for i in range(2)]
        g_full = sbuf("g_full", [P, KD, P], f32)
        mins = sbuf("mins", [P, BLOCKS], f32)
        lowest = sbuf("lowest", [P, 1], f32)
        total = sbuf("total", [P, 1], f32)
        inverse = sbuf("inverse", [P, 1], f32)
        row_sum = sbuf("row_sum", [P, 1], f32)
        minus_mean = sbuf("minus_mean", [P, 1], f32)
        squares = sbuf("squares", [P, D], f32)
        square_sum = sbuf("square_sum", [P, 1], f32)
        eps = sbuf("eps", [P, 1], f32)
        var_eps = sbuf("var_eps", [P, 1], f32)
        rstd = sbuf("rstd", [P, 1], f32)
        bq_cols = sbuf("bq_cols", [P, KD], f32)
        bk_cols = sbuf("bk_cols", [P, KD], f32)
        bk_rows = sbuf("bk_rows", [P, KD, P], f32)
        c_rows = sbuf("c_rows", [P, D], f32)
        c_bias = sbuf("c_bias", [P, 1], f32)
        r_part = [sbuf(f"r_part{i}", [P, 1], f32) for i in range(2)]
        wv_in = adj_t[0][:, 0:KD * D].rearrange("p (k n) -> p k n", k=KD)
        wk_in = adj_t[1][:, 0:KD * D].rearrange("p (k n) -> p k n", k=KD)
        wq_in = probs[0][:, 0:KD * D].rearrange("p (k n) -> p k n", k=KD)
        WvT = probs[1][:, 0:KD * D].bitcast(f16).rearrange("p (k h n) -> p k h n", k=KD, h=2)

        bank = [ctx.enter_context(nc.psum_tensor(f"bank{i}", [P, BLK], f32)) for i in range(8)]
        score_bank, t_bank, o_bank, g_bank = bank[0:2], bank[2:4], bank[4:6], bank[6:8]
        w_bank = score_bank + g_bank

        wv_loaded, wq_loaded, wk_loaded, biases_loaded = (sem(n) for n in (
            "wv_loaded", "wq_loaded", "wk_loaded", "biases_loaded"))
        x_loaded = [sem(f"x_loaded{i}") for i in range(2)]
        adj_loaded = [sem(f"adj_loaded{i}") for i in range(2)]
        stored = [sem(f"stored{i}") for i in range(2)]
        identity_ready, bk_rows_ready, wv_transposed, wvT_high, wvT_low, c_product, c_ready = (sem(n) for n in (
            "identity_ready", "bk_rows_ready", "wv_transposed", "wvT_high", "wvT_low", "c_product", "c_ready"))
        x_transposed, xT_high, xT_low, r_dot, r_ready, v_product, v_high, v_low = (sem(n) for n in (
            "x_transposed", "xT_high", "xT_low", "r_dot", "r_ready", "v_product", "v_high", "v_low"))
        a_product, a_high, a_low, g_bias_product, g_bias_ready = (sem(n) for n in (
            "a_product", "a_high", "a_low", "g_bias_product", "g_bias_ready"))
        g_product, g_full_ready, g_high, g_low = (sem(n) for n in ("g_product", "g_full_ready", "g_high", "g_low"))
        adj_scaled, scores_ready, scores_taken, filled, block_min, tile_min, bias_ready = (sem(n) for n in (
            "adj_scaled", "scores_ready", "scores_taken", "filled", "block_min", "tile_min", "bias_ready"))
        probs_ready, pT_product, pT_high, pT_low, pv_ready = (sem(n) for n in (
            "probs_ready", "pT_product", "pT_high", "pT_low", "pv_ready"))
        sums_taken, total_ready, inverse_ready, out_taken, resid_added = (sem(n) for n in (
            "sums_taken", "total_ready", "inverse_ready", "out_taken", "resid_added"))
        mean_ready, squares_ready, var_ready, rstd_ready, y_ready = (sem(n) for n in (
            "mean_ready", "squares_ready", "var_ready", "rstd_ready", "y_ready"))

        block = ctx.enter_context(nc.Block())

        def wait(engine, semaphore, value):
            if not isinstance(value, int) or value > 0:
                engine.wait_ge(semaphore, value)

        def tile_of(p, j, lag):
            back = j - lag
            q, rest = divmod(back, STEPS)
            odd, b = divmod(rest, BLOCKS)
            if isinstance(p, int) and p + q < 0:
                return None, odd, b
            return 2 * (p + q) + odd, odd, b

        def exists(t):
            return t is not None and (not isinstance(t, int) or t < TILES)

        @block.sync
        def _(sp):
            def load_x(t, odd, rows, free_after):
                for semaphore, count in free_after:
                    wait(sp, semaphore, count)
                sp.dma_start(x_in[odd][0:rows, :], x[bass.ds(t * P, rows), :]).then_inc(x_loaded[odd], 16)

            def rows_of(t):
                return LAST_ROWS if isinstance(t, int) and t == TILES - 1 else P

            def load_chunk(c, odd):
                load_x(c, odd, rows_of(c), [(x_transposed, c - 1), (r_dot, c - 1)])

            def weights(w):
                return w.rearrange("(k p) n -> p k n", p=P)

            sp.dma_start(wv_in, weights(w_v)).then_inc(wv_loaded, 16)
            load_chunk(0, 0)
            sp.dma_start(bq_cols[:, :], b_q.rearrange("(k p) -> p k", p=P),
                         allow_slow_non_contiguous=True).then_inc(biases_loaded, 16)
            sp.dma_start(bk_cols[:, :], b_k.rearrange("(k p) -> p k", p=P),
                         allow_slow_non_contiguous=True).then_inc(biases_loaded, 16)
            sp.dma_start(wq_in, weights(w_q)).then_inc(wq_loaded, 16)
            load_chunk(1, 1)
            sp.dma_start(bv_rows[:, :], b_v.rearrange("(a n) -> a n", a=1).broadcast_to([P, D])
                         ).then_inc(biases_loaded, 16)
            load_chunk(2, 0)
            load_chunk(3, 1)
            sp.dma_start(wk_in, weights(w_k)).then_inc(wk_loaded, 16)
            with sp.Fori(2, PAIRS - 1) as p:
                load_chunk(2 * p, 0)
                load_chunk(2 * p + 1, 1)
            load_chunk(TILES - 2, 0)
            load_chunk(TILES - 1, 1)

            def load_adj(t, odd):
                rows = rows_of(t)
                wait(sp, scores_taken, BLOCKS * (t - 1))
                sp.dma_start(adj_t[odd][0:rows, 0:N], adj[bass.ds(t * P, rows), :]).then_inc(adj_loaded[odd], 16)

            def load_residual(t, odd):
                free = [(resid_added, t - 1)]
                if isinstance(t, int) and t < 2:
                    free = [(x_transposed, TILES), (r_dot, TILES)]
                load_x(t, odd, rows_of(t), free)

            def store(t, odd):
                rows = rows_of(t)
                wait(sp, y_ready, t + 1)
                sp.dma_start(out[bass.ds(t * P, rows), :], y[odd][0:rows, :]).then_inc(stored[odd], 16)

            def sp_pair(p):
                for odd in range(2):
                    t = 2 * p + odd
                    if not isinstance(p, int) or 2 <= t < TILES + 2:
                        load_residual(t - 2, odd)
                    if not isinstance(p, int) or 4 <= t < TILES + 4:
                        store(t - 4, odd)
                    if not isinstance(p, int) or t < TILES:
                        load_adj(t, odd)

            sp.wait_ge(wv_transposed, KD)
            load_adj(0, 0)
            sp.wait_ge(a_product, KD)
            sp.wait_ge(g_bias_product, 1)
            load_adj(1, 1)
            sp_pair(1)
            with sp.Fori(2, PAIRS - 1) as p:
                sp_pair(p)
            for p in range(PAIRS - 1, PAIRS + 2):
                sp_pair(p)
            for odd in range(2):
                sp.wait_ge(stored[odd], 16 * PAIRS)

        @block.gpsimd
        def _(pool):
            nc.gpsimd.memset(identity[:, :], 0.0).then_inc(identity_ready, 1)
            nc.gpsimd.memset(minus_half[:, :], -0.5).then_inc(identity_ready, 1)
            nc.gpsimd.memset(eps[:, :], EPS).then_inc(identity_ready, 1)
            pool.wait_ge(identity_ready, 3)
            nc.gpsimd.affine_select(out=identity[:, :], in_=identity[:, :], compare_op=ALU.not_equal, fill=1.0,
                                    base=0, pattern=[[-1, P]], channel_multiplier=1).then_inc(identity_ready, 1)
            with pool.Fori(0, TILES) as t:
                pool.wait_ge(var_ready, t + 1)
                nc.gpsimd.tensor_tensor(rstd[:, :], var_eps[:, :], minus_half[:, :], ALU.pow).then_inc(rstd_ready, 1)

        @block.scalar
        def _(act):
            def copy(dst, src, scale=1.0):
                return nc.scalar.activation(dst, src, ACT.Copy, scale=scale)

            for k in range(KD):
                act.wait_ge(wv_transposed, k + 1)
                copy(WvT[:, k, 0, :], w_bank[k][:, :], WV_SCALE).then_inc(wvT_high, 1)
            act.wait_ge(c_product, 1)
            copy(c_rows[:, :], o_bank[0][:, :], G_SCALE).then_inc(c_ready, 1)
            copy(c_bias[:, :], o_bank[1][:, 0:1], G_SCALE).then_inc(c_ready, 1)
            act.wait_ge(c_ready, 2)

            def take_transposed_x(c, odd):
                act.wait_ge(x_transposed, c + 1)
                copy(xT[:, :, 0, bass.ds(c * P, P)], t_bank[odd][:, :].rearrange("p (k n) -> p k n", k=KD)
                     ).then_inc(xT_high, 1)

            def finish_r(c, odd):
                act.wait_ge(r_dot, c + 1)
                nc.scalar.activation(r_all[:, bass.ds(c, 1)], r_part[odd][:, :], ACT.Identity,
                                     bias=c_bias[:, :]).then_inc(r_ready, 1)

            def take_v(c, odd):
                act.wait_ge(v_product, c + 1)
                copy(V[:, bass.ds(c, 1), 0, :].rearrange("p a n -> p (a n)"), o_bank[odd][:, :], V_SCALE / WV_SCALE
                     ).then_inc(v_high, 1)

            def prepare_pair(p):
                for odd in range(2):
                    c = 2 * p + odd
                    if not isinstance(p, int) or c + 1 < TILES:
                        take_transposed_x(c + 1, 1 - odd)
                        finish_r(c + 1, 1 - odd)
                    take_v(c, odd)

            take_transposed_x(0, 0)
            finish_r(0, 0)
            with act.Fori(0, PAIRS - 1) as p:
                prepare_pair(p)
            prepare_pair(PAIRS - 1)

            for k in range(KD):
                act.wait_ge(a_product, k + 1)
                copy(A[:, k, 0, :], w_bank[k][:, :], A_SCALE).then_inc(a_high, 1)
            act.wait_ge(g_bias_product, 1)
            copy(g_bias[:, :], t_bank[0][:, 0:KD], G_SCALE).then_inc(g_bias_ready, 1)
            act.wait_ge(g_bias_ready, 1)

            def take_g(p, odd):
                t = 2 * p + odd
                act.wait_ge(g_product, p + 1)
                wait(act, g_low, t)
                if odd:
                    wait(act, scores_ready, STEPS * p)
                for k in range(KD):
                    col = (k % 2) * 2 * P + odd * P
                    nc.scalar.activation(g_full[:, k, :], g_bank[k // 2][:, col:col + P], ACT.Identity,
                                         bias=g_bias[:, k:k + 1], scale=G_SCALE / A_SCALE).then_inc(g_full_ready, 1)
                act.wait_ge(g_full_ready, KD * (t + 1))
                copy(G[odd][:, :, 0, :], g_full[:, :, :]).then_inc(g_high, 1)

            def scale_adj(t, odd, b):
                if b == 0:
                    act.wait_ge(adj_loaded[odd], 8 * (t - odd) + 16)
                cols = slice(b * BLK, b * BLK + width[b])
                copy(adj_t[odd][:, cols], adj_t[odd][:, cols], KAPPA).then_inc(adj_scaled, 1)

            def exponentials(t, odd, b):
                if b == 0:
                    act.wait_ge(bias_ready, t + 1)
                    wait(act, sums_taken, t - 1)
                cols = slice(b * BLK, b * BLK + width[b])
                nc.scalar.activation(probs[odd][:, cols], probs[odd][:, cols], ACT.Exp, bias=exp_bias[odd][:, :],
                                     scale=-FILL, accum_out=sums[odd][:, b:b + 1]).then_inc(probs_ready, 1)

            def take_transposed_probs(t, odd, b):
                u = BLOCKS * t + b
                act.wait_ge(pT_product, u + 1)
                wait(act, pv_ready, u - 1)
                s2 = (odd + b) % 2
                w = chunks[b] * P
                copy(pT[s2][:, 0, 0:w], t_bank[s2][:, 0:w]).then_inc(pT_high, 1)

            def square(t, odd):
                act.wait_ge(mean_ready, t + 1)
                nc.scalar.activation(squares[:, :], y[odd][:, :], ACT.Square, bias=minus_mean[:, :],
                                     accum_out=square_sum[:, :]).then_inc(squares_ready, 1)
                act.wait_ge(squares_ready, t + 1)
                nc.scalar.activation(var_eps[:, :], square_sum[:, :], ACT.Identity, scale=1.0 / D, bias=eps[:, :]
                                     ).then_inc(var_ready, 1)

            take_g(0, 0)
            take_g(0, 1)
            for b in range(BLOCKS):
                scale_adj(0, 0, b)

            def act_step(p, j):
                if j == 1 and not (isinstance(p, int) and (p == 0 or p >= PAIRS)):
                    take_g(p, 1)
                t, odd, b = tile_of(p, j, LAG_E)
                if exists(t):
                    exponentials(t, odd, b)
                t, odd, b = tile_of(p, j, LAG_T)
                if exists(t):
                    take_transposed_probs(t, odd, b)
                t, odd, b = tile_of(p, j, -BLOCKS)
                if exists(t):
                    scale_adj(t, odd, b)
                t, odd, b = tile_of(p, j, LAG_N)
                if exists(t) and b == 1:
                    square(t, odd)
                if j == G_STEP + 1 and not (isinstance(p, int) and p + 1 >= PAIRS):
                    take_g(p + 1, 0)

            for j in range(STEPS):
                act_step(0, j)
            with act.Fori(1, PAIRS - 1) as p:
                for j in range(STEPS):
                    act_step(p, j)
            for j in range(STEPS):
                act_step(PAIRS - 1, j)
            for j in range(STEPS):
                act_step(PAIRS, j)

        @block.vector
        def _(dve):
            nc.vector.memset(bk_rows[:, :, :], 1.0).then_inc(bk_rows_ready, 1)
            nc.vector.memset(probs[0][:, N:NP], 0.0)
            nc.vector.memset(probs[1][:, N:NP], 0.0)
            dve.wait_ge(bk_rows_ready, 1)
            dve.wait_ge(biases_loaded, 48)
            for k in range(KD):
                nc.vector.tensor_scalar(bk_rows[:, k, :], bk_rows[:, k, :], bk_cols[:, k:k + 1], None, ALU.mult
                                        ).then_inc(bk_rows_ready, 1)
            for k in range(KD):
                dve.wait_ge(wvT_high, k + 1)
                nc.vector.scalar_tensor_tensor(out=WvT[:, k, 1, :], in0=w_bank[k][:, :], scalar=WV_SCALE,
                                               in1=WvT[:, k, 0, :], op0=ALU.mult, op1=ALU.subtract
                                               ).then_inc(wvT_low, 1)

            def take_transposed_x(c, odd):
                dve.wait_ge(xT_high, c + 1)
                nc.vector.tensor_tensor(xT[:, :, 1, bass.ds(c * P, P)],
                                        t_bank[odd][:, :].rearrange("p (k n) -> p k n", k=KD),
                                        xT[:, :, 0, bass.ds(c * P, P)], ALU.subtract).then_inc(xT_low, 1)

            def dot_r(c, odd):
                wait(dve, r_ready, c - 1)
                dve.wait_ge(x_loaded[odd], 8 * (c - odd) + 16)
                nc.vector.tensor_tensor_reduce(out=y[odd][:, :], in0=x_in[odd][:, :], in1=c_rows[:, :], scale=1.0,
                                               scalar=0.0, op0=ALU.mult, op1=ALU.add, accum_out=r_part[odd][:, :]
                                               ).then_inc(r_dot, 1)

            def take_v(c, odd):
                dve.wait_ge(v_high, c + 1)
                row = bass.ds(c, 1)
                nc.vector.scalar_tensor_tensor(out=V[:, row, 1, :].rearrange("p a n -> p (a n)"),
                                               in0=o_bank[odd][:, :], scalar=V_SCALE / WV_SCALE,
                                               in1=V[:, row, 0, :].rearrange("p a n -> p (a n)"),
                                               op0=ALU.mult, op1=ALU.subtract).then_inc(v_low, 1)

            def prepare_pair(p):
                for odd in range(2):
                    c = 2 * p + odd
                    if not isinstance(p, int) or c + 1 < TILES:
                        take_transposed_x(c + 1, 1 - odd)
                        dot_r(c + 1, 1 - odd)
                    take_v(c, odd)

            dve.wait_ge(c_ready, 2)
            take_transposed_x(0, 0)
            dot_r(0, 0)
            prepare_pair(0)
            with dve.Fori(1, PAIRS - 1) as p:
                prepare_pair(p)
            prepare_pair(PAIRS - 1)
            for k in range(KD):
                dve.wait_ge(a_high, k + 1)
                nc.vector.scalar_tensor_tensor(out=A[:, k, 1, :], in0=w_bank[k][:, :], scalar=A_SCALE,
                                               in1=A[:, k, 0, :], op0=ALU.mult, op1=ALU.subtract).then_inc(a_low, 1)
            dve.wait_ge(r_ready, TILES)

            def take_g(t, odd):
                dve.wait_ge(g_high, t + 1)
                nc.vector.tensor_tensor(G[odd][:, :, 1, :], g_full[:, :, :], G[odd][:, :, 0, :], ALU.subtract
                                        ).then_inc(g_low, 1)

            def fill_scores(t, odd, b):
                s = BLOCKS * t + b
                w = width[b]
                cols = slice(b * BLK, b * BLK + w)
                dve.wait_ge(scores_ready, s + 1)
                dve.wait_ge(adj_scaled, s + 1)
                u = probs[odd][:, cols]
                nc.vector.scalar_tensor_tensor(out=u, in0=score_bank[(odd + b) % 2][:, 0:w],
                                               scalar=r_all[:, bass.ds(t, 1)], in1=adj_t[odd][:, cols],
                                               op0=ALU.add, op1=ALU.mult).then_inc(scores_taken, 1)
                dve.wait_ge(scores_taken, s + 1)
                nc.vector.scalar_tensor_tensor(out=u, in0=u, scalar=0.0, in1=u, op0=ALU.is_equal,
                                               op1=ALU.subtract).then_inc(filled, 1)

            def minimum(t, odd, b):
                s = BLOCKS * t + b
                cols = slice(b * BLK, b * BLK + width[b])
                dve.wait_ge(filled, s + 1)
                nc.vector.tensor_reduce(mins[:, b:b + 1], probs[odd][:, cols], axis=AX.X, op=ALU.min
                                        ).then_inc(block_min, 1)
                if b == BLOCKS - 1:
                    dve.wait_ge(block_min, s + 1)
                    nc.vector.tensor_reduce(lowest[:, :], mins[:, :], axis=AX.X, op=ALU.min).then_inc(tile_min, 1)
                    dve.wait_ge(tile_min, t + 1)
                    nc.vector.tensor_scalar(exp_bias[odd][:, :], lowest[:, :], FILL, P_SHIFT, ALU.mult, ALU.add
                                            ).then_inc(bias_ready, 1)

            def take_transposed_probs(t, odd, b):
                u = BLOCKS * t + b
                dve.wait_ge(pT_high, u + 1)
                s2 = (odd + b) % 2
                w = chunks[b] * P
                nc.vector.tensor_tensor(pT[s2][:, 1, 0:w], t_bank[s2][:, 0:w], pT[s2][:, 0, 0:w], ALU.subtract
                                        ).then_inc(pT_low, 1)

            def finish_tile(t, odd):
                dve.wait_ge(probs_ready, BLOCKS * (t + 1))
                nc.vector.tensor_reduce(total[:, :], sums[odd][:, :], axis=AX.X, op=ALU.add).then_inc(sums_taken, 1)
                dve.wait_ge(sums_taken, t + 1)
                nc.vector.tensor_scalar(total[:, :], total[:, :], V_SCALE, None, ALU.mult).then_inc(total_ready, 1)
                dve.wait_ge(total_ready, t + 1)
                nc.vector.reciprocal(inverse[:, :], total[:, :]).then_inc(inverse_ready, 1)
                dve.wait_ge(inverse_ready, t + 1)
                dve.wait_ge(pv_ready, BLOCKS * (t + 1))
                wait(dve, stored[odd], 8 * (t - odd))
                nc.vector.scalar_tensor_tensor(out=y[odd][:, :], in0=o_bank[odd][:, :], scalar=inverse[:, :],
                                               in1=bv_rows[:, :], op0=ALU.mult, op1=ALU.add).then_inc(out_taken, 1)
                dve.wait_ge(out_taken, t + 1)
                dve.wait_ge(x_loaded[odd], 16 * PAIRS + 8 * (t - odd) + 16)
                nc.vector.scalar_tensor_tensor(out=y[odd][:, :], in0=y[odd][:, :], scalar=0.0, in1=x_in[odd][:, :],
                                               op0=ALU.max, op1=ALU.add, accum_out=row_sum[:, :]).then_inc(resid_added, 1)
                dve.wait_ge(resid_added, t + 1)
                nc.vector.tensor_scalar(minus_mean[:, :], row_sum[:, :], -1.0 / D, None, ALU.mult
                                        ).then_inc(mean_ready, 1)

            def normalise(t, odd):
                dve.wait_ge(rstd_ready, t + 1)
                nc.vector.tensor_scalar(y[odd][:, :], y[odd][:, :], minus_mean[:, :], rstd[:, :], ALU.add,
                                        ALU.mult).then_inc(y_ready, 1)

            take_g(0, 0)
            take_g(1, 1)

            def dve_step(p, j):
                now, odd, b = tile_of(p, j, 0)
                if exists(now):
                    fill_scores(now, odd, b)
                before, odd_before, b_before = tile_of(p, j, LAG_T)
                if exists(before):
                    take_transposed_probs(before, odd_before, b_before)
                if exists(now):
                    minimum(now, odd, b)
                if j == 1 and not (isinstance(p, int) and (p == 0 or p >= PAIRS)):
                    take_g(2 * p + 1, 1)
                if j == G_STEP + 1 and not (isinstance(p, int) and p + 1 >= PAIRS):
                    take_g(2 * p + 2, 0)
                t, odd, b = tile_of(p, j, LAG_N)
                if exists(t) and b == 0:
                    finish_tile(t, odd)
                if exists(t) and b == 2:
                    normalise(t, odd)

            for j in range(STEPS):
                dve_step(0, j)
            with dve.Fori(1, PAIRS - 1) as p:
                for j in range(STEPS):
                    dve_step(p, j)
            for j in range(STEPS):
                dve_step(PAIRS - 1, j)
            for j in range(STEPS):
                dve_step(PAIRS, j)

        @block.tensor
        def _(pe):
            def product(dst, lhs, rhs, n, j):
                nc.tensor.matmul(dst, lhs[0], rhs[0], start=(j == 0), stop=False)
                nc.tensor.matmul(dst, lhs[0], rhs[1], start=False, stop=False)
                return nc.tensor.matmul(dst, lhs[1], rhs[0], start=False, stop=(j == n - 1))

            pe.wait_ge(identity_ready, 4)
            pe.wait_ge(wv_loaded, 16)
            for k in range(KD):
                for m in range(KD):
                    last = nc.tensor.transpose(w_bank[k][:, m * P:(m + 1) * P], wv_in[:, m, k * P:(k + 1) * P],
                                               identity[:, :])
                last.then_inc(wv_transposed, 1)

            pe.wait_ge(wq_loaded, 16)
            pe.wait_ge(bk_rows_ready, 1 + KD)
            for k in range(KD):
                nc.tensor.matmul(o_bank[0][:, :], bk_rows[:, k, :], wq_in[:, k, :], start=(k == 0), stop=(k == KD - 1))
            for k in range(KD):
                last = nc.tensor.matmul(o_bank[1][:, 0:1], bk_rows[:, k, :], bq_cols[:, k:k + 1], start=(k == 0),
                                        stop=(k == KD - 1))
            last.then_inc(c_product, 1)

            def transpose_x(c, odd):
                pe.wait_ge(x_loaded[odd], 8 * (c - odd) + 16)
                wait(pe, xT_low, c - 1)
                for k in range(KD):
                    last = nc.tensor.transpose(t_bank[odd][:, k * P:(k + 1) * P], x_in[odd][:, k * P:(k + 1) * P],
                                               identity[:, :])
                last.then_inc(x_transposed, 1)

            def v_rows(c, odd):
                pe.wait_ge(xT_low, c + 1)
                if isinstance(c, int) and c == 0:
                    pe.wait_ge(wvT_low, KD)
                if isinstance(c, int) and c < 2:
                    pe.wait_ge(c_ready, 2)
                wait(pe, v_low, c - 1)
                nodes = bass.ds(c * P, P)
                for k in range(KD):
                    last = product(o_bank[odd][:, :], (xT[:, k, 0, nodes], xT[:, k, 1, nodes]),
                                   (WvT[:, k, 0, :], WvT[:, k, 1, :]), KD, k)
                last.then_inc(v_product, 1)

            def prepare_pair(p):
                for odd in range(2):
                    c = 2 * p + odd
                    if not isinstance(p, int) or c + 1 < TILES:
                        transpose_x(c + 1, 1 - odd)
                    v_rows(c, odd)

            transpose_x(0, 0)
            prepare_pair(0)
            with pe.Fori(1, PAIRS - 1) as p:
                prepare_pair(p)
            prepare_pair(PAIRS - 1)

            pe.wait_ge(wk_loaded, 16)
            for m in range(KD):
                for k in range(KD):
                    last = nc.tensor.matmul(w_bank[m][:, :], wq_in[:, k, m * P:(m + 1) * P], wk_in[:, k, :],
                                            start=(k == 0), stop=(k == KD - 1))
                last.then_inc(a_product, 1)
            for m in range(KD):
                for k in range(KD):
                    last = nc.tensor.matmul(t_bank[0][:, m:m + 1], wk_in[:, k, m * P:(m + 1) * P], bq_cols[:, k:k + 1],
                                            start=(k == 0), stop=(k == KD - 1))
            last.then_inc(g_bias_product, 1)
            pe.wait_ge(a_low, KD)

            def g_columns(p):
                nodes = bass.ds(p * 2 * P, 2 * P)
                for m in range(KD):
                    cols = slice((m % 2) * 2 * P, (m % 2 + 1) * 2 * P)
                    for k in range(KD):
                        at = slice(m * P, (m + 1) * P)
                        last = product(g_bank[m // 2][:, cols], (A[:, k, 0, at], A[:, k, 1, at]),
                                       (xT[:, k, 0, nodes], xT[:, k, 1, nodes]), KD, k)
                last.then_inc(g_product, 1)

            def scores(t, odd, b):
                s = BLOCKS * t + b
                if b == 0:
                    pe.wait_ge(g_low, t + 1)
                wait(pe, scores_taken, s - 1)
                nodes = slice(b * BLK, b * BLK + width[b])
                for k in range(KD):
                    last = product(score_bank[(odd + b) % 2][:, 0:width[b]], (G[odd][:, k, 0, :], G[odd][:, k, 1, :]),
                                   (xT[:, k, 0, nodes], xT[:, k, 1, nodes]), KD, k)
                last.then_inc(scores_ready, 1)

            def transpose_probs(t, odd, b):
                u = BLOCKS * t + b
                pe.wait_ge(probs_ready, u + 1)
                wait(pe, pT_low, u - 1)
                for i in range(chunks[b]):
                    at = slice(b * BLK + i * P, b * BLK + (i + 1) * P)
                    last = nc.tensor.transpose(t_bank[(odd + b) % 2][:, i * P:(i + 1) * P], probs[odd][:, at],
                                               identity[:, :])
                last.then_inc(pT_product, 1)

            def times_v(t, odd, b):
                u = BLOCKS * t + b
                pe.wait_ge(pT_low, u + 1)
                if b == 0:
                    wait(pe, out_taken, t - 1)
                half = pT[(odd + b) % 2]
                for i in range(chunks[b]):
                    c = b * (BLK // P) + i
                    last = product(o_bank[odd][:, :], (half[:, 0, i * P:(i + 1) * P], half[:, 1, i * P:(i + 1) * P]),
                                   (V[:, c, 0, :], V[:, c, 1, :]), TILES, c)
                last.then_inc(pv_ready, 1)

            g_columns(0)
            pe.wait_ge(v_low, TILES)
            pe.wait_ge(g_bias_ready, 1)

            def pe_step(p, j):
                t, odd, b = tile_of(p, j, 0)
                if exists(t):
                    scores(t, odd, b)
                if j == G_STEP and not (isinstance(p, int) and p + 1 >= PAIRS):
                    g_columns(p + 1)
                t, odd, b = tile_of(p, j, LAG_T)
                if exists(t):
                    transpose_probs(t, odd, b)
                t, odd, b = tile_of(p, j, LAG_V)
                if exists(t):
                    times_v(t, odd, b)

            for j in range(STEPS):
                pe_step(0, j)
            with pe.Fori(1, PAIRS - 1) as p:
                for j in range(STEPS):
                    pe_step(p, j)
            for j in range(STEPS):
                pe_step(PAIRS - 1, j)
            for j in range(LAG_V):
                pe_step(PAIRS, j)


_INS = ['x', 'adj', 'L0_gnn_W_q', 'L0_gnn_b_q', 'L0_gnn_W_k', 'L0_gnn_b_k', 'L0_gnn_W_v', 'L0_gnn_b_v']
_OUTS = [((3327, 512), 'float32')]


def kernel(**inputs):
    import numpy as _np
    import concourse.bacc as _bacc
    from concourse import mybir as _mybir
    from concourse.bass_utils import run_bass_kernel_spmd as _run

    nc = _bacc.Bacc("TRN2", target_bir_lowering=False, num_devices=1)
    arrays, args = {}, []
    for name in _INS:
        a = _np.ascontiguousarray(inputs[name])
        arrays[f"in_{name}_dram"] = a
        args.append(nc.dram_tensor(f"in_{name}_dram", a.shape, _mybir.dt.from_np(a.dtype), kind="ExternalInput").ap())
    for i, (shape, dtype) in enumerate(_OUTS):
        dt = _mybir.dt.from_np(_np.dtype(dtype))
        args.append(nc.dram_tensor(f"out_{i}_dram", shape, dt, kind="ExternalOutput").ap())
    graph_attention_kernel(nc, *args)
    r = _run(nc, [arrays], core_ids=[0])
    got = tuple(r.results[0][f"out_{i}_dram"] for i in range(len(_OUTS)))
    return got[0]
```

```python
import math

import concourse.bass as bass
from concourse import mybir
from contextlib import ExitStack

P = 128


def graph_attention_kernel(nc, x, adj, w_q, b_q, w_k, b_k, w_v, b_v, out):
    f32, f16, u32 = mybir.dt.float32, mybir.dt.float16, mybir.dt.uint32
    ALU, ACT, AX = mybir.AluOpType, mybir.ActivationFunctionType, mybir.AxisListType

    N, D = x.shape
    KD = D // P
    TILES = -(-N // P)
    LAST_ROWS = N - (TILES - 1) * P
    PAIRS = TILES // 2
    NP = TILES * P
    BLK = 512
    BLOCKS = -(-N // BLK)
    width = [min(BLK, N - b * BLK) for b in range(BLOCKS)]
    chunks = [-(-w // P) for w in width]
    NB = BLOCKS * BLK
    STEPS = 2 * BLOCKS
    LAG_V = 2 * BLOCKS
    LAG_E, LAG_T = BLOCKS, BLOCKS + 1
    SOFTMAX = [tuple(range(b, min(b + 2, BLOCKS))) for b in range(0, BLOCKS, 2)]
    Q = 32
    QUADS = P // Q
    GROUPS = [(0, BLOCKS // 2 + 1), (BLOCKS // 2 + 1, BLOCKS)]
    MOVED = 16 * QUADS * (QUADS - 1)
    KEEP_STEPS = [LAG_T + 3, 2 * BLOCKS]
    LAG_N = LAG_V + BLOCKS
    G_STEP, G_EVEN_STEP, G_ODD_STEP = BLOCKS + 4, BLOCKS + 5, 4
    assert TILES % 2 == 0 and BLOCKS % 2 == 1 and D == BLK

    WV_SCALE, V_SCALE, A_SCALE, G_SCALE = 2.0 ** 8, 2.0 ** 4, 2.0 ** 10, 2.0 ** 4
    FILL = 10000.0
    KAPPA = 1.0 / (math.sqrt(D) * FILL * G_SCALE)
    P_SHIFT = 13 * math.log(2.0)
    EPS = 1e-5

    ctx = ExitStack()
    with ctx:
        def sbuf(name, shape, dt):
            return ctx.enter_context(nc.sbuf_tensor(name, shape, dt))

        def sem(name):
            return ctx.enter_context(nc.semaphore(name))

        xT = sbuf("xT", [P, KD, 2, NP], f16)
        V = sbuf("V", [P, TILES, 2, D], f16)
        A = sbuf("A", [P, KD, 2, D], f16)
        r_all = sbuf("r_all", [P, TILES], f32)
        bv_rows = sbuf("bv_rows", [P, D], f32)
        identity = sbuf("identity", [P, P], f32)
        g_bias = sbuf("g_bias", [P, KD], f32)
        minus_half = sbuf("minus_half", [P, 1], f32)
        adj_t = [sbuf(f"adj_t{i}", [P, N], f32) for i in range(2)]
        probs = [sbuf(f"probs{i}", [P, NB], f32) for i in range(2)]
        x_in = [sbuf(f"x_in{i}", [P, D], f32) for i in range(2)]
        y = [sbuf(f"y{i}", [P, D], f32) for i in range(2)]
        G = [sbuf(f"G{i}", [P, KD, 2, P], f16) for i in range(2)]
        exp_bias = [sbuf(f"exp_bias{i}", [P, 1], f32) for i in range(2)]
        sums = [sbuf(f"sums{i}", [P, BLOCKS], f32) for i in range(2)]
        pairs = [sbuf(f"pairs{i}", [P, BLK, 2], f16) for i in range(2)]
        pairs_last = sbuf("pairs_last", [P, BLK, 2], f16)
        pT = sbuf("pT", [P, NB, 2], f16)
        g_full = sbuf("g_full", [P, KD, P], f32)
        mins = sbuf("mins", [P, BLOCKS], f32)
        lowest = sbuf("lowest", [P, 1], f32)
        total = sbuf("total", [P, 1], f32)
        inverse = sbuf("inverse", [P, 1], f32)
        row_sum = sbuf("row_sum", [P, 1], f32)
        minus_mean = sbuf("minus_mean", [P, 1], f32)
        square_sum = sbuf("square_sum", [P, 1], f32)
        eps = sbuf("eps", [P, 1], f32)
        var_eps = sbuf("var_eps", [P, 1], f32)
        rstd = sbuf("rstd", [P, 1], f32)
        bq_cols = sbuf("bq_cols", [P, KD], f32)
        bk_cols = sbuf("bk_cols", [P, KD], f32)
        c_rows = sbuf("c_rows", [P, D], f32)
        c_bias = sbuf("c_bias", [P, 1], f32)
        r_part = [sbuf(f"r_part{i}", [P, 1], f32) for i in range(2)]
        wv_in = adj_t[0][:, 0:KD * D].rearrange("p (k n) -> p k n", k=KD)
        wk_in = adj_t[1][:, 0:KD * D].rearrange("p (k n) -> p k n", k=KD)
        wq_in = probs[0][:, 0:KD * D].rearrange("p (k n) -> p k n", k=KD)
        bk_rows = pairs[0][:, :, :].rearrange("p n h -> p (n h)").bitcast(f32).rearrange(
            "p (k n) -> p k n", k=KD)
        WvT = probs[1][:, 0:KD * D].bitcast(f16).rearrange("p (k h n) -> p k h n", k=KD, h=2)

        bank = [ctx.enter_context(nc.psum_tensor(f"bank{i}", [P, BLK], f32)) for i in range(8)]
        score_bank, t_bank, o_bank, g_bank = bank[0:2], bank[2:4], bank[4:6], bank[6:8]
        deviations = t_bank[0]
        w_bank = score_bank + g_bank

        wk_loaded, biases_loaded, bv_loaded = (sem(n) for n in ("wk_loaded", "biases_loaded", "bv_loaded"))
        wq_loaded = [sem(f"wq_loaded{m}") for m in range(KD)]
        wv_loaded = [sem(f"wv_loaded{m}") for m in range(KD)]
        x_loaded = [sem(f"x_loaded{i}") for i in range(2)]
        adj_loaded = [sem(f"adj_loaded{i}") for i in range(2)]
        stored = [sem(f"stored{i}") for i in range(2)]
        identity_ready, bk_rows_ready, wv_transposed, wvT_high, wvT_low, c_product, c_ready = (sem(n) for n in (
            "identity_ready", "bk_rows_ready", "wv_transposed", "wvT_high", "wvT_low", "c_product", "c_ready"))
        x_transposed, xT_high, xT_low, r_dot, r_ready, v_product, v_high, v_low = (sem(n) for n in (
            "x_transposed", "xT_high", "xT_low", "r_dot", "r_ready", "v_product", "v_high", "v_low"))
        a_product, a_high, a_low, g_bias_product, g_bias_ready = (sem(n) for n in (
            "a_product", "a_high", "a_low", "g_bias_product", "g_bias_ready"))
        g_product, g_full_ready, g_high, g_low = (sem(n) for n in ("g_product", "g_full_ready", "g_high", "g_low"))
        adj_scaled, scores_ready, scores_taken, filled, block_min, tile_min, bias_ready = (sem(n) for n in (
            "adj_scaled", "scores_ready", "scores_taken", "filled", "block_min", "tile_min", "bias_ready"))
        probs_ready, pair_high, pair_low, pairs_turned = (sem(n) for n in (
            "probs_ready", "pair_high", "pair_low", "pairs_turned"))
        group_turned = [sem(f"group_turned{g}") for g in range(len(GROUPS))]
        pT_free = [sem(f"pT_free{g}") for g in range(len(GROUPS))]
        squares_kept = [sem(f"squares_kept{g}") for g in range(len(GROUPS))]
        squares_moved = [sem(f"squares_moved{g}") for g in range(len(GROUPS))]
        sums_taken, total_ready, inverse_ready, out_taken, resid_added = (sem(n) for n in (
            "sums_taken", "total_ready", "inverse_ready", "out_taken", "resid_added"))
        mean_ready, squares_ready, var_ready, rstd_ready, y_ready = (sem(n) for n in (
            "mean_ready", "squares_ready", "var_ready", "rstd_ready", "y_ready"))

        A_ORDER = [*range(1, KD), 0]

        block = ctx.enter_context(nc.Block())

        def wait(engine, semaphore, value):
            if not isinstance(value, int) or value > 0:
                engine.wait_ge(semaphore, value)

        def tile_of(p, j, lag):
            back = j - lag
            q, rest = divmod(back, STEPS)
            odd, b = divmod(rest, BLOCKS)
            if isinstance(p, int) and p + q < 0:
                return None, odd, b
            return 2 * (p + q) + odd, odd, b

        def pairs_of(odd, b):
            return pairs_last if b == BLOCKS - 1 else pairs[(odd + b) % 2]

        def squares(odd, g, i, j):
            first, end = GROUPS[g]
            cols, n = slice(first * BLK, end * BLK), BLK // QUADS
            turned = probs[odd][:, cols].rearrange("p (b n) -> p b n", n=BLK)
            moved = pT[:, cols, :].rearrange("p n h -> p (n h)").bitcast(f32).rearrange("p (b n) -> p b n", n=BLK)
            return (moved[j * Q:(j + 1) * Q, :, i * n:(i + 1) * n], turned[i * Q:(i + 1) * Q, :, j * n:(j + 1) * n])

        def softmax_blocks(p, j, lag):
            t, odd, i = tile_of(p, j, lag)
            return t, odd, SOFTMAX[i] if exists(t) and i < len(SOFTMAX) else ()

        def exists(t):
            return t is not None and (not isinstance(t, int) or t < TILES)

        @block.sync
        def _(sp):
            def load_x(t, odd, rows, free_after):
                for semaphore, count in free_after:
                    wait(sp, semaphore, count)
                sp.dma_start(x_in[odd][0:rows, :], x[bass.ds(t * P, rows), :]).then_inc(x_loaded[odd], 16)

            def rows_of(t):
                return LAST_ROWS if isinstance(t, int) and t == TILES - 1 else P

            def load_chunk(c, odd):
                load_x(c, odd, rows_of(c), [(x_transposed, c - 1), (r_dot, c - 1)])

            load_chunk(0, 0)
            sp.dma_start(bk_cols[:, :], b_k.rearrange("(k p) -> p k", p=P),
                         allow_slow_non_contiguous=True).then_inc(biases_loaded, 16)
            sp.dma_start(bq_cols[:, :], b_q.rearrange("(k p) -> p k", p=P),
                         allow_slow_non_contiguous=True).then_inc(biases_loaded, 16)
            load_chunk(1, 1)
            for m in range(KD):
                sp.dma_start(wq_in[:, m, :], w_q[m * P:(m + 1) * P, :]).then_inc(wq_loaded[m], 16)
            for m in range(KD):
                sp.dma_start(wv_in[:, m, :], w_v[m * P:(m + 1) * P, :]).then_inc(wv_loaded[m], 16)
            sp.dma_start(bv_rows[:, :], b_v.rearrange("(a n) -> a n", a=1).broadcast_to([P, D])
                         ).then_inc(bv_loaded, 16)
            load_chunk(2, 0)
            load_chunk(3, 1)
            sp.dma_start(wk_in, w_k.rearrange("(k p) n -> p k n", p=P)).then_inc(wk_loaded, 16)
            with sp.Fori(2, PAIRS - 1) as p:
                load_chunk(2 * p, 0)
                load_chunk(2 * p + 1, 1)
            load_chunk(TILES - 2, 0)
            load_chunk(TILES - 1, 1)

            def load_adj(t, odd):
                rows = rows_of(t)
                wait(sp, scores_taken, BLOCKS * (t - 1))
                sp.dma_start(adj_t[odd][0:rows, 0:N], adj[bass.ds(t * P, rows), :]).then_inc(adj_loaded[odd], 16)

            def load_residual(t, odd):
                free = [(resid_added, t - 1)]
                if isinstance(t, int) and t < 2:
                    free = [(x_transposed, TILES), (r_dot, TILES)]
                load_x(t, odd, rows_of(t), free)

            def store(t, odd):
                rows = rows_of(t)
                wait(sp, y_ready, t + 1)
                sp.dma_start(out[bass.ds(t * P, rows), :], y[odd][0:rows, :]).then_inc(stored[odd], 16)

            def move_squares(t, odd, g):
                sp.wait_ge(group_turned[g], t + 1)
                sp.wait_ge(pT_free[g], t + 1)
                for i in range(QUADS):
                    for j in range(QUADS):
                        if i != j:
                            sp.dma_start(*squares(odd, g, i, j)).then_inc(squares_moved[g], 16)

            def sp_step(p, j):
                t, odd, b = tile_of(p, j, BLOCKS)
                if exists(t) and b == 0 and (not isinstance(t, int) or t + 2 < TILES):
                    load_adj(t + 2, odd)
                t, odd, blocks = softmax_blocks(p, j, LAG_T)
                for g, (_, end) in enumerate(GROUPS):
                    if end - 1 in blocks:
                        move_squares(t, odd, g)
                t, odd, b = tile_of(p, j, LAG_N)
                if exists(t) and b == 3:
                    store(t, odd)
                    if not isinstance(t, int) or t + 2 < TILES:
                        load_residual(t + 2, odd)

            sp.wait_ge(wv_transposed, KD)
            load_adj(0, 0)
            load_residual(0, 0)
            load_residual(1, 1)
            sp.wait_ge(a_product, KD)
            sp.wait_ge(g_bias_product, 1)
            load_adj(1, 1)
            for free in pT_free:
                sp.sem_inc(free, 1)
            for p in range(2):
                for j in range(STEPS):
                    sp_step(p, j)
            with sp.Fori(2, PAIRS - 1) as p:
                for j in range(STEPS):
                    sp_step(p, j)
            for p in range(PAIRS - 1, PAIRS + 2):
                for j in range(STEPS):
                    sp_step(p, j)
            for odd in range(2):
                sp.wait_ge(stored[odd], 16 * PAIRS)

        @block.gpsimd
        def _(pool):
            nc.gpsimd.memset(identity[:, :], 0.0).then_inc(identity_ready, 1)
            nc.gpsimd.memset(minus_half[:, :], -0.5).then_inc(identity_ready, 1)
            nc.gpsimd.memset(eps[:, :], EPS).then_inc(identity_ready, 1)
            pool.wait_ge(identity_ready, 3)
            nc.gpsimd.affine_select(out=identity[:, :], in_=identity[:, :], compare_op=ALU.not_equal, fill=1.0,
                                    base=0, pattern=[[-1, P]], channel_multiplier=1).then_inc(identity_ready, 1)
            with pool.Fori(0, TILES) as t:
                pool.wait_ge(var_ready, t + 1)
                nc.gpsimd.tensor_tensor(rstd[:, :], var_eps[:, :], minus_half[:, :], ALU.pow).then_inc(rstd_ready, 1)

        @block.scalar
        def _(act):
            def copy(dst, src, scale=1.0):
                return nc.scalar.activation(dst, src, ACT.Copy, scale=scale)

            def take_transposed_x(c, odd):
                act.wait_ge(x_transposed, c + 1)
                copy(xT[:, :, 0, bass.ds(c * P, P)], t_bank[odd][:, :].rearrange("p (k n) -> p k n", k=KD)
                     ).then_inc(xT_high, 1)

            def finish_r(c, odd):
                act.wait_ge(r_dot, c + 1)
                nc.scalar.activation(r_all[:, bass.ds(c, 1)], r_part[odd][:, :], ACT.Identity,
                                     bias=c_bias[:, :]).then_inc(r_ready, 1)

            def take_v(c, odd):
                act.wait_ge(v_product, c + 1)
                copy(V[:, bass.ds(c, 1), 0, :].rearrange("p a n -> p (a n)"), o_bank[odd][:, :], V_SCALE / WV_SCALE
                     ).then_inc(v_high, 1)

            def prepare_pair(p):
                for odd in range(2):
                    c = 2 * p + odd
                    if not isinstance(c, int) or c > 0:
                        take_transposed_x(c + 1, 1 - odd)
                        finish_r(c + 1, 1 - odd)
                    take_v(c, odd)

            for c in range(2):
                take_transposed_x(c, c)
            act.wait_ge(c_product, 1)
            copy(c_rows[:, :], o_bank[0][:, :], G_SCALE).then_inc(c_ready, 1)
            copy(c_bias[:, :], o_bank[1][:, 0:1], G_SCALE).then_inc(c_ready, 1)
            act.wait_ge(c_ready, 2)
            for c in range(2):
                finish_r(c, c)
            for k in range(KD):
                act.wait_ge(wv_transposed, k + 1)
                copy(WvT[:, k, 0, :], w_bank[k][:, :], WV_SCALE).then_inc(wvT_high, 1)
            prepare_pair(0)
            with act.Fori(1, PAIRS - 1) as p:
                prepare_pair(p)

            act.wait_ge(g_bias_product, 1)
            copy(g_bias[:, :], w_bank[0][:, 0:KD], G_SCALE).then_inc(g_bias_ready, 1)
            for k in A_ORDER:
                act.wait_ge(a_product, A_ORDER.index(k) + 1)
                copy(A[:, k, 0, :], w_bank[k][:, :], A_SCALE).then_inc(a_high, 1)
            act.wait_ge(g_bias_ready, 1)

            def take_g(p, odd):
                t = 2 * p + odd
                act.wait_ge(g_product, p + 1)
                wait(act, g_low, t)
                if odd:
                    wait(act, scores_ready, STEPS * p)
                for k in range(KD):
                    col = (k % 2) * 2 * P + odd * P
                    nc.scalar.activation(g_full[:, k, :], g_bank[k // 2][:, col:col + P], ACT.Identity,
                                         bias=g_bias[:, k:k + 1], scale=G_SCALE / A_SCALE).then_inc(g_full_ready, 1)
                act.wait_ge(g_full_ready, KD * (t + 1))
                copy(G[odd][:, :, 0, :], g_full[:, :, :]).then_inc(g_high, 1)

            def scale_adj(t, odd, b):
                if b == 0:
                    act.wait_ge(adj_loaded[odd], 8 * (t - odd) + 16)
                cols = slice(b * BLK, b * BLK + width[b])
                copy(adj_t[odd][:, cols], adj_t[odd][:, cols], KAPPA).then_inc(adj_scaled, 1)

            def exponentials(t, odd, b):
                if b == 0:
                    act.wait_ge(bias_ready, t + 1)
                    wait(act, sums_taken, t - 1)
                cols = slice(b * BLK, b * BLK + width[b])
                nc.scalar.activation(probs[odd][:, cols], probs[odd][:, cols], ACT.Exp, bias=exp_bias[odd][:, :],
                                     scale=-FILL, accum_out=sums[odd][:, b:b + 1]).then_inc(probs_ready, 1)

            def high_halves(t, odd, b):
                u = BLOCKS * t + b
                act.wait_ge(probs_ready, u + 1)
                wait(act, pairs_turned, u - 1)
                copy(pairs_of(odd, b)[:, 0:width[b], 0], probs[odd][:, b * BLK:b * BLK + width[b]]
                     ).then_inc(pair_high, 1)

            def square(t, odd):
                act.wait_ge(mean_ready, t + 1)
                nc.scalar.activation(deviations[:, :], y[odd][:, :], ACT.Square, bias=minus_mean[:, :],
                                     accum_out=square_sum[:, :]).then_inc(squares_ready, 1)
                act.wait_ge(squares_ready, t + 1)
                nc.scalar.activation(var_eps[:, :], square_sum[:, :], ACT.Identity, scale=1.0 / D, bias=eps[:, :]
                                     ).then_inc(var_ready, 1)

            take_transposed_x(TILES - 1, 1)
            finish_r(TILES - 1, 1)
            take_v(TILES - 2, 0)
            take_g(0, 0)
            take_g(0, 1)
            take_v(TILES - 1, 1)
            for b in range(BLOCKS):
                scale_adj(0, 0, b)

            def act_step(p, j):
                if j == G_ODD_STEP and not (isinstance(p, int) and (p == 0 or p >= PAIRS)):
                    take_g(p, 1)
                t, odd, blocks = softmax_blocks(p, j, LAG_E)
                for b in blocks:
                    exponentials(t, odd, b)
                for b in blocks:
                    high_halves(t, odd, b)
                t, odd, b = tile_of(p, j, -BLOCKS)
                if exists(t):
                    scale_adj(t, odd, b)
                t, odd, b = tile_of(p, j, LAG_N)
                if exists(t) and b == 1:
                    square(t, odd)
                if j == G_EVEN_STEP and not (isinstance(p, int) and p + 1 >= PAIRS):
                    take_g(p + 1, 0)

            for p in range(2):
                for j in range(STEPS):
                    act_step(p, j)
            with act.Fori(2, PAIRS - 1) as p:
                for j in range(STEPS):
                    act_step(p, j)
            for p in range(PAIRS - 1, PAIRS + 2):
                for j in range(STEPS):
                    act_step(p, j)

        @block.vector
        def _(dve):
            nc.vector.memset(bk_rows[:, :, :], 1.0).then_inc(bk_rows_ready, 1)
            nc.vector.memset(pairs_last[:, width[-1]:, :], 0.0)
            dve.wait_ge(bk_rows_ready, 1)
            dve.wait_ge(biases_loaded, 32)
            for k in range(KD):
                nc.vector.tensor_scalar(bk_rows[:, k, :], bk_rows[:, k, :], bk_cols[:, k:k + 1], None, ALU.mult
                                        ).then_inc(bk_rows_ready, 1)

            def take_transposed_x(c, odd):
                dve.wait_ge(xT_high, c + 1)
                nc.vector.tensor_tensor(xT[:, :, 1, bass.ds(c * P, P)],
                                        t_bank[odd][:, :].rearrange("p (k n) -> p k n", k=KD),
                                        xT[:, :, 0, bass.ds(c * P, P)], ALU.subtract).then_inc(xT_low, 1)

            def dot_r(c, odd):
                wait(dve, r_ready, c - 1)
                dve.wait_ge(x_loaded[odd], 8 * (c - odd) + 16)
                nc.vector.tensor_tensor_reduce(out=y[odd][:, :], in0=x_in[odd][:, :], in1=c_rows[:, :], scale=1.0,
                                               scalar=0.0, op0=ALU.mult, op1=ALU.add, accum_out=r_part[odd][:, :]
                                               ).then_inc(r_dot, 1)

            def take_v(c, odd):
                dve.wait_ge(v_high, c + 1)
                row = bass.ds(c, 1)
                nc.vector.scalar_tensor_tensor(out=V[:, row, 1, :].rearrange("p a n -> p (a n)"),
                                               in0=o_bank[odd][:, :], scalar=V_SCALE / WV_SCALE,
                                               in1=V[:, row, 0, :].rearrange("p a n -> p (a n)"),
                                               op0=ALU.mult, op1=ALU.subtract).then_inc(v_low, 1)

            def prepare_pair(p):
                for odd in range(2):
                    c = 2 * p + odd
                    if not isinstance(c, int) or c > 0:
                        take_transposed_x(c + 1, 1 - odd)
                        dot_r(c + 1, 1 - odd)
                    take_v(c, odd)

            for c in range(2):
                take_transposed_x(c, c)
            dve.wait_ge(c_ready, 2)
            for c in range(2):
                dot_r(c, c)
            for k in range(KD):
                dve.wait_ge(wvT_high, k + 1)
                nc.vector.scalar_tensor_tensor(out=WvT[:, k, 1, :], in0=w_bank[k][:, :], scalar=WV_SCALE,
                                               in1=WvT[:, k, 0, :], op0=ALU.mult, op1=ALU.subtract
                                               ).then_inc(wvT_low, 1)
            prepare_pair(0)
            with dve.Fori(1, PAIRS - 1) as p:
                prepare_pair(p)
            for k in A_ORDER:
                dve.wait_ge(a_high, A_ORDER.index(k) + 1)
                nc.vector.scalar_tensor_tensor(out=A[:, k, 1, :], in0=w_bank[k][:, :], scalar=A_SCALE,
                                               in1=A[:, k, 0, :], op0=ALU.mult, op1=ALU.subtract).then_inc(a_low, 1)

            def take_g(t, odd):
                dve.wait_ge(g_high, t + 1)
                nc.vector.tensor_tensor(G[odd][:, :, 1, :], g_full[:, :, :], G[odd][:, :, 0, :], ALU.subtract
                                        ).then_inc(g_low, 1)

            def fill_scores(t, odd, b):
                s = BLOCKS * t + b
                w = width[b]
                cols = slice(b * BLK, b * BLK + w)
                dve.wait_ge(scores_ready, s + 1)
                dve.wait_ge(adj_scaled, s + 1)
                for g, (first, _) in enumerate(GROUPS):
                    if b == first:
                        wait(dve, squares_moved[g], MOVED * (t - 1))
                u = probs[odd][:, cols]
                nc.vector.scalar_tensor_tensor(out=u, in0=score_bank[(odd + b) % 2][:, 0:w],
                                               scalar=r_all[:, bass.ds(t, 1)], in1=adj_t[odd][:, cols],
                                               op0=ALU.add, op1=ALU.mult).then_inc(scores_taken, 1)
                dve.wait_ge(scores_taken, s + 1)
                nc.vector.scalar_tensor_tensor(out=u, in0=u, scalar=0.0, in1=u, op0=ALU.is_equal,
                                               op1=ALU.subtract).then_inc(filled, 1)

            def minimum(t, odd, b):
                s = BLOCKS * t + b
                cols = slice(b * BLK, b * BLK + width[b])
                dve.wait_ge(filled, s + 1)
                nc.vector.tensor_reduce(mins[:, b:b + 1], probs[odd][:, cols], axis=AX.X, op=ALU.min
                                        ).then_inc(block_min, 1)
                if b == BLOCKS - 1:
                    dve.wait_ge(block_min, s + 1)
                    nc.vector.tensor_reduce(lowest[:, :], mins[:, :], axis=AX.X, op=ALU.min).then_inc(tile_min, 1)
                    dve.wait_ge(tile_min, t + 1)
                    nc.vector.tensor_scalar(exp_bias[odd][:, :], lowest[:, :], FILL, P_SHIFT, ALU.mult, ALU.add
                                            ).then_inc(bias_ready, 1)

            def low_halves(t, odd, b):
                dve.wait_ge(pair_high, BLOCKS * t + b + 1)
                own = pairs_of(odd, b)
                nc.vector.tensor_tensor(own[:, 0:width[b], 1], probs[odd][:, b * BLK:b * BLK + width[b]],
                                        own[:, 0:width[b], 0], ALU.subtract).then_inc(pair_low, 1)

            def turn_squares(t, odd, b):
                dve.wait_ge(pair_low, BLOCKS * t + b + 1)
                words = pairs_of(odd, b)[:, :, :].rearrange("p n h -> p (n h)").bitcast(u32)
                turned = probs[odd][:, b * BLK:(b + 1) * BLK].bitcast(u32)
                nc.vector.transpose(turned.rearrange("p (q n c) -> p c q n", q=QUADS, n=Q),
                                    words.rearrange("p (c q n) -> p c q n", q=QUADS, n=Q)).then_inc(pairs_turned, 1)
                for g, (_, end) in enumerate(GROUPS):
                    if b == end - 1:
                        dve.wait_ge(pairs_turned, BLOCKS * t + end)
                        dve.sem_inc(group_turned[g], 1)

            def keep_squares(t, odd, g):
                dve.wait_ge(group_turned[g], t + 1)
                dve.wait_ge(pT_free[g], t + 1)
                for i in range(QUADS):
                    dst, src = squares(odd, g, i, i)
                    last = nc.vector.tensor_copy(dst, src)
                last.then_inc(squares_kept[g], 1)

            def finish_tile(t, odd):
                dve.wait_ge(probs_ready, BLOCKS * (t + 1))
                nc.vector.tensor_reduce(total[:, :], sums[odd][:, :], axis=AX.X, op=ALU.add).then_inc(sums_taken, 1)
                dve.wait_ge(sums_taken, t + 1)
                nc.vector.tensor_scalar(total[:, :], total[:, :], V_SCALE, None, ALU.mult).then_inc(total_ready, 1)
                dve.wait_ge(total_ready, t + 1)
                nc.vector.reciprocal(inverse[:, :], total[:, :]).then_inc(inverse_ready, 1)
                dve.wait_ge(inverse_ready, t + 1)
                dve.wait_ge(pT_free[-1], t + 2)
                wait(dve, stored[odd], 8 * (t - odd))
                if isinstance(t, int) and t == 0:
                    dve.wait_ge(bv_loaded, 16)
                nc.vector.scalar_tensor_tensor(out=y[odd][:, :], in0=o_bank[odd][:, :], scalar=inverse[:, :],
                                               in1=bv_rows[:, :], op0=ALU.mult, op1=ALU.add).then_inc(out_taken, 1)
                dve.wait_ge(out_taken, t + 1)
                dve.wait_ge(x_loaded[odd], 16 * PAIRS + 8 * (t - odd) + 16)
                nc.vector.scalar_tensor_tensor(out=y[odd][:, :], in0=y[odd][:, :], scalar=0.0, in1=x_in[odd][:, :],
                                               op0=ALU.max, op1=ALU.add, accum_out=row_sum[:, :]).then_inc(resid_added, 1)
                dve.wait_ge(resid_added, t + 1)
                nc.vector.tensor_scalar(minus_mean[:, :], row_sum[:, :], -1.0 / D, None, ALU.mult
                                        ).then_inc(mean_ready, 1)

            def normalise(t, odd):
                dve.wait_ge(rstd_ready, t + 1)
                nc.vector.tensor_scalar(y[odd][:, :], y[odd][:, :], minus_mean[:, :], rstd[:, :], ALU.add,
                                        ALU.mult).then_inc(y_ready, 1)

            take_transposed_x(TILES - 1, 1)
            dot_r(TILES - 1, 1)
            take_v(TILES - 2, 0)
            take_g(0, 0)
            take_g(1, 1)
            take_v(TILES - 1, 1)
            dve.wait_ge(r_ready, TILES)

            def dve_step(p, j):
                now, odd, b = tile_of(p, j, 0)
                if exists(now):
                    fill_scores(now, odd, b)
                before, odd_before, blocks = softmax_blocks(p, j, LAG_T)
                for b_before in blocks:
                    low_halves(before, odd_before, b_before)
                for b_before in blocks:
                    turn_squares(before, odd_before, b_before)
                if exists(now):
                    minimum(now, odd, b)
                for g, lag in enumerate(KEEP_STEPS):
                    t, odd_t, b_t = tile_of(p, j, lag)
                    if exists(t) and b_t == 0:
                        keep_squares(t, odd_t, g)
                if j == G_ODD_STEP and not (isinstance(p, int) and (p == 0 or p >= PAIRS)):
                    take_g(2 * p + 1, 1)
                if j == G_EVEN_STEP and not (isinstance(p, int) and p + 1 >= PAIRS):
                    take_g(2 * p + 2, 0)
                t, odd, b = tile_of(p, j, LAG_N)
                if exists(t) and b == 0:
                    finish_tile(t, odd)
                if exists(t) and b == 2:
                    normalise(t, odd)

            for p in range(2):
                for j in range(STEPS):
                    dve_step(p, j)
            with dve.Fori(2, PAIRS - 1) as p:
                for j in range(STEPS):
                    dve_step(p, j)
            for p in range(PAIRS - 1, PAIRS + 2):
                for j in range(STEPS):
                    dve_step(p, j)

        @block.tensor
        def _(pe):
            def product(dst, lhs, rhs, n, j):
                nc.tensor.matmul(dst, lhs[0], rhs[0], start=(j == 0), stop=False)
                nc.tensor.matmul(dst, lhs[0], rhs[1], start=False, stop=False)
                return nc.tensor.matmul(dst, lhs[1], rhs[0], start=False, stop=(j == n - 1))

            def transpose_x(c, odd):
                pe.wait_ge(x_loaded[odd], 8 * (c - odd) + 16)
                wait(pe, xT_low, c - 1)
                for k in range(KD):
                    last = nc.tensor.transpose(t_bank[odd][:, k * P:(k + 1) * P], x_in[odd][:, k * P:(k + 1) * P],
                                               identity[:, :])
                last.then_inc(x_transposed, 1)

            def v_rows(c, odd):
                pe.wait_ge(xT_low, c + 1)
                if isinstance(c, int) and c == 0:
                    pe.wait_ge(c_ready, 2)
                wait(pe, v_low, c - 1)
                nodes = bass.ds(c * P, P)
                for k in range(KD):
                    if isinstance(c, int) and c == 0:
                        pe.wait_ge(wvT_low, k + 1)
                    last = product(o_bank[odd][:, :], (xT[:, k, 0, nodes], xT[:, k, 1, nodes]),
                                   (WvT[:, k, 0, :], WvT[:, k, 1, :]), KD, k)
                last.then_inc(v_product, 1)

            def prepare_pair(p):
                for odd in range(2):
                    c = 2 * p + odd
                    if not isinstance(c, int) or c > 0:
                        transpose_x(c + 1, 1 - odd)
                    v_rows(c, odd)

            pe.wait_ge(identity_ready, 4)
            for c in range(2):
                transpose_x(c, c)

            pe.wait_ge(bk_rows_ready, 1 + KD)
            for k in range(KD):
                pe.wait_ge(wq_loaded[k], 16)
                nc.tensor.matmul(o_bank[0][:, :], bk_rows[:, k, :], wq_in[:, k, :], start=(k == 0), stop=(k == KD - 1))
            for k in range(KD):
                last = nc.tensor.matmul(o_bank[1][:, 0:1], bk_rows[:, k, :], bq_cols[:, k:k + 1], start=(k == 0),
                                        stop=(k == KD - 1))
            last.then_inc(c_product, 1)

            for m in range(KD):
                pe.wait_ge(wv_loaded[m], 16)
                for k in range(KD):
                    last = nc.tensor.transpose(w_bank[k][:, m * P:(m + 1) * P], wv_in[:, m, k * P:(k + 1) * P],
                                               identity[:, :])
                    if m == KD - 1:
                        last.then_inc(wv_transposed, 1)

            prepare_pair(0)
            with pe.Fori(1, PAIRS - 1) as p:
                prepare_pair(p)

            pe.wait_ge(wk_loaded, 16)
            for m in range(KD):
                for k in range(KD):
                    last = nc.tensor.matmul(w_bank[0][:, m:m + 1], wk_in[:, k, m * P:(m + 1) * P], bq_cols[:, k:k + 1],
                                            start=(k == 0), stop=(k == KD - 1))
            last.then_inc(g_bias_product, 1)
            for m in A_ORDER:
                if m == 0:
                    pe.wait_ge(g_bias_ready, 1)
                for k in range(KD):
                    last = nc.tensor.matmul(w_bank[m][:, :], wq_in[:, k, m * P:(m + 1) * P], wk_in[:, k, :],
                                            start=(k == 0), stop=(k == KD - 1))
                last.then_inc(a_product, 1)

            def g_columns(p):
                nodes = bass.ds(p * 2 * P, 2 * P)
                for m in range(KD):
                    cols = slice((m % 2) * 2 * P, (m % 2 + 1) * 2 * P)
                    for k in range(KD):
                        at = slice(m * P, (m + 1) * P)
                        last = product(g_bank[m // 2][:, cols], (A[:, k, 0, at], A[:, k, 1, at]),
                                       (xT[:, k, 0, nodes], xT[:, k, 1, nodes]), KD, k)
                last.then_inc(g_product, 1)

            def scores(t, odd, b):
                s = BLOCKS * t + b
                if b == 0:
                    pe.wait_ge(g_low, t + 1)
                wait(pe, scores_taken, s - 1)
                nodes = slice(b * BLK, b * BLK + width[b])
                for k in range(KD):
                    last = product(score_bank[(odd + b) % 2][:, 0:width[b]], (G[odd][:, k, 0, :], G[odd][:, k, 1, :]),
                                   (xT[:, k, 0, nodes], xT[:, k, 1, nodes]), KD, k)
                last.then_inc(scores_ready, 1)

            def times_v(t, odd, b):
                for g, (first, _) in enumerate(GROUPS):
                    if b == first:
                        pe.wait_ge(squares_moved[g], MOVED * (t + 1))
                        pe.wait_ge(squares_kept[g], t + 1)
                if b == 0:
                    wait(pe, out_taken, t - 1)
                if b == 0 and isinstance(t, int) and t == 0:
                    pe.wait_ge(v_low, TILES)
                high, low = (pT[:, b * BLK:(b + 1) * BLK, h].rearrange("p (i c) -> p c i", i=P) for h in range(2))
                for i in range(chunks[b]):
                    c = b * (BLK // P) + i
                    last = product(o_bank[odd][:, :], (high[:, i, :], low[:, i, :]),
                                   (V[:, c, 0, :], V[:, c, 1, :]), TILES, c)
                for g, (_, end) in enumerate(GROUPS):
                    if b == end - 1:
                        last.then_inc(pT_free[g], 1)

            transpose_x(TILES - 1, 1)
            v_rows(TILES - 2, 0)
            pe.wait_ge(a_low, KD)
            g_columns(0)
            v_rows(TILES - 1, 1)

            def pe_step(p, j):
                t, odd, b = tile_of(p, j, 0)
                if exists(t):
                    scores(t, odd, b)
                if j == G_STEP and not (isinstance(p, int) and p + 1 >= PAIRS):
                    g_columns(p + 1)
                t, odd, b = tile_of(p, j, LAG_V)
                if exists(t):
                    times_v(t, odd, b)

            for p in range(2):
                for j in range(STEPS):
                    pe_step(p, j)
            with pe.Fori(2, PAIRS - 1) as p:
                for j in range(STEPS):
                    pe_step(p, j)
            for p in range(PAIRS - 1, PAIRS + 2):
                for j in range(STEPS):
                    pe_step(p, j)


_INS = ['x', 'adj', 'L0_gnn_W_q', 'L0_gnn_b_q', 'L0_gnn_W_k', 'L0_gnn_b_k', 'L0_gnn_W_v', 'L0_gnn_b_v']
_OUTS = [((3327, 512), 'float32')]


def kernel(**inputs):
    import numpy as _np
    import concourse.bacc as _bacc
    from concourse import mybir as _mybir
    from concourse.bass_utils import run_bass_kernel_spmd as _run

    nc = _bacc.Bacc("TRN2", target_bir_lowering=False, num_devices=1)
    arrays, args = {}, []
    for name in _INS:
        a = _np.ascontiguousarray(inputs[name])
        arrays[f"in_{name}_dram"] = a
        args.append(nc.dram_tensor(f"in_{name}_dram", a.shape, _mybir.dt.from_np(a.dtype), kind="ExternalInput").ap())
    for i, (shape, dtype) in enumerate(_OUTS):
        dt = _mybir.dt.from_np(_np.dtype(dtype))
        args.append(nc.dram_tensor(f"out_{i}_dram", shape, dt, kind="ExternalOutput").ap())
    graph_attention_kernel(nc, *args)
    r = _run(nc, [arrays], core_ids=[0])
    got = tuple(r.results[0][f"out_{i}_dram"] for i in range(len(_OUTS)))
    return got[0]
```
